# Optimizing a Trainium2 kernel written in Bass

```python
import numpy as np
import jax
import jax.numpy as jnp

def _softmax(x, axis=-1):
    return jax.nn.softmax(x, axis=axis)
def _gelu(x):
    return jax.nn.gelu(x, approximate=True)
def _silu(x):
    return jax.nn.silu(x)
def _sigmoid(x):
    return jax.nn.sigmoid(x)
def _layernorm(x, axis=-1, eps=1e-5):
    m = jnp.mean(x, axis=axis, keepdims=True)
    v = jnp.var(x, axis=axis, keepdims=True)
    return (x - m) / jnp.sqrt(v + eps)
def _scatter_add(tgt, idx, src, axis=0):
    return tgt.at[idx].add(src)
def _segment_sum(src, seg, n):
    return jax.ops.segment_sum(src, seg, n)

kernel_name = 'mk_rec_standalone_d1_rec_57976f'

def setup_inputs(seed: int = 0):
    np.random.seed(seed)
    _w = jnp.asarray
    def _rec_inputs():
        import jax
        import jax.numpy as jnp
        _rk = jax.random.key(seed)
        r_x = 7.22013e-05 + 1.00017 * jax.random.normal(jax.random.fold_in(_rk, 1), (4096, 32, 64), jnp.float32)
        return r_x
    r_x = _rec_inputs()
    def _L0_rec_setup():
        import jax, jax.numpy as jnp
        import numpy as np
        from itertools import combinations
        NUM_FIELDS = 32
        DIM = 64
        BATCH = 4096
        _PAIRS = np.array(list(combinations(range(NUM_FIELDS), 2)), dtype=np.int32)
        IDX_I = jnp.asarray(_PAIRS[:, 0])
        IDX_J = jnp.asarray(_PAIRS[:, 1])
        key = jax.random.key(seed)
        k1, k2 = jax.random.split(key)
        P = _PAIRS.shape[0]
        x = jax.random.normal(k1, (BATCH, NUM_FIELDS, DIM), dtype=jnp.float32)
        W = jax.random.normal(k2, (P, DIM, DIM), dtype=jnp.float32) * (1.0 / np.sqrt(DIM))
        return {'x': x, 'W': W}
    _L0_rec_all = _L0_rec_setup()
    _L0_rec_in = {k: v for k, v in _L0_rec_all.items() if k in ('W', )}
    del _L0_rec_all

    return {
        "r_x": r_x,
        "L0_rec_W": _L0_rec_in["W"],
    }

def reference(r_x, L0_rec_W):
    import jax
    import jax.numpy as jnp
    def _L0_rec_ref(x, W):
        import jax, jax.numpy as jnp
        import numpy as np
        from itertools import combinations
        NUM_FIELDS = 32
        DIM = 64
        BATCH = 4096
        _PAIRS = np.array(list(combinations(range(NUM_FIELDS), 2)), dtype=np.int32)
        IDX_I = jnp.asarray(_PAIRS[:, 0])
        IDX_J = jnp.asarray(_PAIRS[:, 1])
        xi = x[:, IDX_I, :]
        xj = x[:, IDX_J, :]
        out = jnp.einsum('bpd,ped->bpe', xi, W) * xj
        return out

    y = _L0_rec_ref(r_x, L0_rec_W)
    return y


_drawn_inputs = setup_inputs


def setup_inputs(seed=0):
    import zlib

    import numpy as np

    out = dict(_drawn_inputs(seed))
    spreads = {}
    factors = {}
    for name, (base, spread) in spreads.items():
        noise = np.random.default_rng([zlib.crc32(name.encode()), seed]).standard_normal(out[name].shape)
        drawn = base * np.exp(spread * noise) if base else spread * noise
        out[name] = jnp.asarray(drawn.astype(out[name].dtype))
    for name, factor in factors.items():
        out[name] = (out[name] * factor).astype(out[name].dtype)
    return out
```

```python
from contextlib import ExitStack

import concourse.bass as bass
from concourse import mybir


def field_interaction_kernel(nc: bass.Bass, x_dram: bass.AP, w_dram: bass.AP, out_dram: bass.AP):
    fp32 = mybir.dt.float32
    fp32r = mybir.dt.float32r
    ALU = mybir.AluOpType

    P = 128
    BATCH, FIELDS, DIM = x_dram.shape
    PAIRS = w_dram.shape[0]
    TILES = BATCH // P
    SENDERS = FIELDS - 1
    assert PAIRS == FIELDS * (FIELDS - 1) // 2 and 2 * DIM == P and BATCH % (2 * P) == 0

    BANK = 512
    BANK_PAIRS = BANK // DIM
    CHUNK_PAIRS = 2 * BANK_PAIRS
    GROUPS = 16
    GROUP_PAIRS = PAIRS // GROUPS
    GROUP_COLS = GROUP_PAIRS * DIM
    CHUNKS = 2 * GROUPS
    assert PAIRS == GROUPS * GROUP_PAIRS and CHUNK_PAIRS < GROUP_PAIRS <= 2 * CHUNK_PAIRS
    PSUM_SLOTS = 3
    STORE_SLOTS = 4
    assert GROUPS % STORE_SLOTS == 0

    FILL_FIELDS = BANK // P
    FILLS = -(-SENDERS // FILL_FIELDS)
    FILL_SLOTS = 4
    FILL_BANKS = 2
    AHEAD = 2
    assert FILLS % FILL_SLOTS == 0 and AHEAD <= FILL_BANKS

    PIECES = 4
    PIECE_FILLS = FILLS // PIECES
    PIECE_FIELDS = PIECE_FILLS * FILL_FIELDS

    W_RUN = 8
    W_ROWS = P * W_RUN
    W_BLOCKS = PAIRS * DIM // W_ROWS
    W_LOADS = 6
    W_SPLITS = 3
    assert W_BLOCKS * W_ROWS == PAIRS * DIM and W_LOADS % W_SPLITS == 0
    W_LOOPS, W_REST = divmod(W_BLOCKS, W_LOADS)

    first_pair = [i * (2 * FIELDS - i - 1) // 2 for i in range(FIELDS)]

    def chunk_pairs(c):
        start = c // 2 * GROUP_PAIRS + c % 2 * CHUNK_PAIRS
        return start, min(start + CHUNK_PAIRS, (c // 2 + 1) * GROUP_PAIRS)

    def runs(start, end):
        found = []
        for i in range(SENDERS):
            a, b = max(start, first_pair[i]), min(end, first_pair[i + 1])
            if a < b:
                found.append((i, a, b - a))
        return found

    def fields_of(fill):
        return range(fill * FILL_FIELDS, min((fill + 1) * FILL_FIELDS, SENDERS))

    last_chunk = [next(c for c in range(CHUNKS) if chunk_pairs(c)[1] >= first_pair[fields_of(n)[-1] + 1])
                  for n in range(FILLS)]

    def piece(p):
        return slice(p * PIECE_FIELDS, min((p + 1) * PIECE_FIELDS, SENDERS))

    x_view = x_dram.rearrange("b f d -> b (f d)")
    out_view = out_dram.rearrange("b p e -> b (p e)")
    w_view = w_dram.rearrange("p e d -> (p e) d").rearrange("(q r) d -> q (r d)", r=W_RUN)

    ctx = ExitStack()
    with ctx:
        def sbuf(name, shape, dtype=fp32):
            return ctx.enter_context(nc.sbuf_tensor(name, shape, dtype))

        def sem(name):
            return ctx.enter_context(nc.semaphore(name))

        w_t = sbuf("w_t", [P, PAIRS * DIM], fp32r)
        x_rows = sbuf("x_rows", [P, 2, FIELDS, DIM])
        x_split = sbuf("x_split", [P, SENDERS, 2, DIM])
        STRAIGHT, CROSSED = 0, 1
        x_t = sbuf("x_t", [P, FILL_SLOTS, 2, FILL_FIELDS * P], fp32r)
        identity = sbuf("identity", [P, P])
        store_ring = sbuf("store_ring", [P, STORE_SLOTS * GROUP_COLS])
        w_raw = store_ring[:, 0:W_LOADS * W_RUN * DIM].rearrange("p (s n) -> p s n", s=W_LOADS)
        w_split = store_ring[:, W_LOADS * W_RUN * DIM:(W_LOADS + 2 * W_SPLITS) * W_RUN * DIM] \
            .rearrange("p (s r h d) -> p s r h d", s=W_SPLITS, r=W_RUN, h=2)

        products = ctx.enter_context(nc.psum_tensor("products", [P, PSUM_SLOTS, 2 * BANK], fp32))
        transposes = ctx.enter_context(nc.psum_tensor("transposes", [P, FILL_BANKS, BANK], fp32))

        identity_zeroed = sem("identity_zeroed")
        identity_ready = sem("identity_ready")
        w_loaded = [sem(f"w_loaded{s}") for s in range(W_LOADS)]
        w_hi_ready = sem("w_hi_ready")
        w_lo_pool = sem("w_lo_pool")
        w_lo_vector = sem("w_lo_vector")
        w_transposed = sem("w_transposed")
        w_out_scalar = sem("w_out_scalar")
        w_out_vector = sem("w_out_vector")
        x_loaded = [sem(f"x_loaded{s}") for s in range(2)]
        x_hi_ready = sem("x_hi_ready")
        x_lo_ready = sem("x_lo_ready")
        fill_transposed = sem("fill_transposed")
        fill_ready = sem("fill_ready")
        chunk_ready = sem("chunk_ready")
        chunk_done = sem("chunk_done")
        stored = [sem(f"stored{s}") for s in range(STORE_SLOTS)]

        block = ctx.enter_context(nc.Block())

        def w_blocks(eng, emit):
            for s in range(W_LOADS):
                emit(s, s, s < W_LOADS)
            with eng.Fori(1, W_LOOPS) as turn:
                for s in range(W_LOADS):
                    emit(turn * W_LOADS + s, s, False)
            for s in range(W_REST):
                emit(W_LOOPS * W_LOADS + s, s, False)

        def w_t_block(b, half):
            r0 = half * W_RUN // 2
            return w_t[:, bass.ds(b * W_ROWS, W_ROWS)].rearrange("p (q r) -> p q r", r=W_RUN)[:, :, r0:r0 + W_RUN // 2]

        def w_transposes(s, half):
            return products[:, s % W_SPLITS, half * BANK:(half + 1) * BANK].rearrange("p (r q) -> p q r", q=P)

        @block.sync
        def _(sp):
            def load_w(b, s, first):
                if not first:
                    sp.wait_ge(w_lo_pool, b - W_LOADS + 1)
                    sp.wait_ge(w_lo_vector, b - W_LOADS + 1)
                sp.dma_start(w_raw[:, s, :], w_view[bass.ds(b * P, P), :]).then_inc(w_loaded[s], 16)

            def load_x(t, s):
                sp.dma_start(x_rows[:, s, :, :].rearrange("p f d -> p (f d)"), x_view[bass.ds(t * P, P), :]).then_inc(x_loaded[s], 16)

            w_blocks(sp, load_w)
            load_x(0, 0)
            load_x(1, 1)

            def store(t):
                for g in range(GROUPS):
                    slot = g % STORE_SLOTS
                    sp.wait_ge(chunk_done, t * CHUNKS + 2 * (g + 1))
                    sp.dma_start(out_view[bass.ds(t * P, P), g * GROUP_COLS:(g + 1) * GROUP_COLS],
                                 store_ring[:, slot * GROUP_COLS:(slot + 1) * GROUP_COLS]).then_inc(stored[slot], 16)

            with sp.Fori(0, TILES // 2 - 1) as k:
                for s in range(2):
                    store(2 * k + s)
                    load_x(2 * k + s + 2, s)
            for t in range(TILES - 2, TILES):
                store(t)
            for slot in range(STORE_SLOTS):
                sp.wait_ge(stored[slot], 16 * TILES * GROUPS // STORE_SLOTS)

        @block.gpsimd
        def _(pool):
            nc.gpsimd.memset(identity[:, :], 0.0).then_inc(identity_zeroed, 1)
            pool.wait_ge(identity_zeroed, 1)
            nc.gpsimd.affine_select(out=identity[:, :], in_=identity[:, :], compare_op=ALU.not_equal, fill=1.0,
                                    base=0, pattern=[[-1, P]], channel_multiplier=1).then_inc(identity_ready, 1)

            def w_lo(b, s, first):
                pool.wait_ge(w_hi_ready, b + 1)
                rows = slice(0, W_RUN // 2)
                raw = w_raw[:, s, :].rearrange("p (r d) -> p r d", r=W_RUN)[:, rows, :]
                split = w_split[:, s % W_SPLITS, rows, :, :]
                nc.gpsimd.tensor_tensor(split[:, :, 1, :], raw, split[:, :, 0, :], ALU.subtract).then_inc(w_lo_pool, 1)

            w_blocks(pool, w_lo)

            def x_lo_of(t, s):
                for p in range(PIECES):
                    pool.wait_ge(x_hi_ready, t * PIECES + p + 1)
                    nc.gpsimd.tensor_tensor(x_split[:, piece(p), 1, :], x_rows[:, s, piece(p), :],
                                            x_split[:, piece(p), 0, :], ALU.subtract).then_inc(x_lo_ready, 1)

            with pool.Fori(0, TILES // 2) as k:
                for s in range(2):
                    x_lo_of(2 * k + s, s)

        @block.scalar
        def _(act):
            def w_out(b, s):
                act.wait_ge(w_transposed, b + 1)
                nc.scalar.copy(w_t_block(b, 1), w_transposes(s, 1)).then_inc(w_out_scalar, 1)

            def w_hi(b, s, first):
                act.wait_ge(w_loaded[s], 16 * (b // W_LOADS + 1) if first else loads_seen[0])
                if not first or s >= W_SPLITS:
                    act.wait_ge(w_transposed, b - W_SPLITS + 1)
                nc.scalar.copy(w_split[:, s % W_SPLITS, :, 0, :].bitcast(fp32r),
                               w_raw[:, s, :].rearrange("p (r d) -> p r d", r=W_RUN)).then_inc(w_hi_ready, 1)
                if not first or s >= 1:
                    w_out(b - 1, (s - 1) % W_LOADS)

            loads_seen = [0]
            for s in range(W_LOADS):
                w_hi(s, s, True)
            with act.Fori(1, W_LOOPS) as turn:
                loads_seen[0] = 16 * (turn + 1)
                for s in range(W_LOADS):
                    w_hi(turn * W_LOADS + s, s, False)
            loads_seen[0] = 16 * (W_LOOPS + 1)
            for s in range(W_REST):
                w_hi(W_LOOPS * W_LOADS + s, s, False)
            w_out(W_BLOCKS - 1, (W_BLOCKS - 1) % W_LOADS)

            def x_hi_of(s, p):
                nc.scalar.copy(x_split[:, piece(p), 0, :].bitcast(fp32r),
                               x_rows[:, s, piece(p), :]).then_inc(x_hi_ready, 1)

            def tile(t, k, s, first, last):
                for n in range(FILLS):
                    slot, cols = n % FILL_SLOTS, len(fields_of(n)) * P
                    act.wait_ge(fill_transposed, t * FILLS + n + 1)
                    if not (first and n < FILL_SLOTS):
                        used = last_chunk[(n - FILL_SLOTS) % FILLS] + 1
                        act.wait_ge(chunk_ready, t * CHUNKS + used - (CHUNKS if n < FILL_SLOTS else 0))
                    for to, start, lane in ((STRAIGHT, 0, P), (CROSSED, 0, DIM), (CROSSED, DIM, DIM)):
                        source = start if to == STRAIGHT else DIM - start
                        last_copy = nc.scalar.copy(x_t[start:start + lane, slot, to, 0:cols],
                                                   transposes[source:source + lane, n % FILL_BANKS, 0:cols])
                    last_copy.then_inc(fill_ready, 1)
                    if (n + 1) % PIECE_FILLS == 0 and not last:
                        if n + 1 == PIECE_FILLS:
                            act.wait_ge(x_loaded[1 - s], 16 * (k + 1 + s))
                        x_hi_of(1 - s, n // PIECE_FILLS)

            act.wait_ge(x_loaded[0], 16)
            for p in range(PIECES):
                x_hi_of(0, p)
            tile(0, 0, 0, True, False)
            with act.Fori(0, TILES // 2 - 1) as k:
                tile(2 * k + 1, k, 1, False, False)
                tile(2 * k + 2, k + 1, 0, False, False)
            tile(TILES - 1, TILES // 2 - 1, 1, False, True)

        @block.vector
        def _(dve):
            def w_out(b, s):
                dve.wait_ge(w_transposed, b + 1)
                nc.vector.tensor_copy(w_t_block(b, 0), w_transposes(s, 0)).then_inc(w_out_vector, 1)

            def w_lo(b, s, first):
                dve.wait_ge(w_hi_ready, b + 1)
                rows = slice(W_RUN // 2, W_RUN)
                raw = w_raw[:, s, :].rearrange("p (r d) -> p r d", r=W_RUN)[:, rows, :]
                split = w_split[:, s % W_SPLITS, rows, :, :]
                nc.vector.tensor_tensor(split[:, :, 1, :], raw, split[:, :, 0, :], ALU.subtract).then_inc(w_lo_vector, 1)
                if not first or s >= 1:
                    w_out(b - 1, (s - 1) % W_LOADS)

            w_blocks(dve, w_lo)
            w_out(W_BLOCKS - 1, (W_BLOCKS - 1) % W_LOADS)

            def tile(t, s, first):
                for c in range(CHUNKS):
                    group = c // 2
                    start, end = chunk_pairs(c)
                    if c % 2 == 0 and not (first and group < STORE_SLOTS):
                        dve.wait_ge(stored[group % STORE_SLOTS],
                                    16 * (GROUPS // STORE_SLOTS * t + group // STORE_SLOTS))
                    dve.wait_ge(chunk_ready, t * CHUNKS + c + 1)
                    for i, pair, count in runs(start, end):
                        j = i + 1 + pair - first_pair[i]
                        at = (group % STORE_SLOTS) * GROUP_COLS + (pair - group * GROUP_PAIRS) * DIM
                        last = nc.vector.tensor_tensor(
                            store_ring[:, at:at + count * DIM],
                            products[:, c % PSUM_SLOTS, (pair - start) * DIM:(pair - start + count) * DIM],
                            x_rows[:, s, j:j + count, :].rearrange("p f d -> p (f d)"), ALU.mult)
                    last.then_inc(chunk_done, 1)

            tile(0, 0, True)
            with dve.Fori(0, TILES // 2 - 1) as k:
                tile(2 * k + 1, 1, False)
                tile(2 * k + 2, 0, False)
            tile(TILES - 1, 1, False)

        @block.tensor
        def _(pe):
            pe.wait_ge(identity_ready, 1)

            def w_transpose(b, s, first):
                pe.wait_ge(w_lo_pool, b + 1)
                pe.wait_ge(w_lo_vector, b + 1)
                if not first or s >= W_SPLITS:
                    pe.wait_ge(w_out_scalar, b - W_SPLITS + 1)
                    pe.wait_ge(w_out_vector, b - W_SPLITS + 1)
                for r in range(W_RUN):
                    last = nc.tensor.transpose(products[:, s % W_SPLITS, r * P:(r + 1) * P],
                                               w_split[:, s % W_SPLITS, r, :, :].rearrange("p h d -> p (h d)"),
                                               identity[:, :])
                last.then_inc(w_transposed, 1)

            w_blocks(pe, w_transpose)
            pe.wait_ge(w_out_scalar, W_BLOCKS)
            pe.wait_ge(w_out_vector, W_BLOCKS)

            def transpose_fill(t, n):
                if n % PIECE_FILLS == 0:
                    pe.wait_ge(x_lo_ready, t * PIECES + n // PIECE_FILLS + 1)
                for f, i in enumerate(fields_of(n)):
                    last = nc.tensor.transpose(transposes[:, n % FILL_BANKS, f * P:(f + 1) * P],
                                               x_split[:, i, :, :].rearrange("p h d -> p (h d)"), identity[:, :])
                last.then_inc(fill_transposed, 1)

            def tile(t, first, last_tile):
                for c in range(CHUNKS):
                    start, end = chunk_pairs(c)
                    slot = c % PSUM_SLOTS
                    if c >= PSUM_SLOTS:
                        pe.wait_ge(chunk_done, t * CHUNKS + c - PSUM_SLOTS + 1)
                    elif not first and c < 2:
                        pe.wait_ge(chunk_done, t * CHUNKS - (1 - c))
                    for bank in range(start, end, BANK_PAIRS):
                        for i, pair, count in runs(bank, min(bank + BANK_PAIRS, end)):
                            n, f = divmod(i, FILL_FIELDS)
                            if pair == first_pair[i] and f == 0:
                                pe.wait_ge(fill_ready, t * FILLS + n + 1)
                                if n + AHEAD < FILLS:
                                    transpose_fill(t, n + AHEAD)
                                elif not last_tile:
                                    transpose_fill(t + 1, n + AHEAD - FILLS)
                            at = (pair - start) * DIM
                            for way in (CROSSED, STRAIGHT):
                                last = nc.tensor.matmul(products[:, slot, at:at + count * DIM],
                                                        x_t[:, n % FILL_SLOTS, way, f * P:(f + 1) * P],
                                                        w_t[:, pair * DIM:(pair + count) * DIM],
                                                        start=way == CROSSED, stop=way == STRAIGHT)
                    last.then_inc(chunk_ready, 1)

            for n in range(AHEAD):
                transpose_fill(0, n)
            tile(0, True, False)
            with pe.Fori(1, TILES - 1) as t:
                tile(t, False, False)
            tile(TILES - 1, False, True)


_INS = ["r_x", "L0_rec_W"]


def kernel(**inputs):
    import numpy as _np
    import concourse.bacc as _bacc
    from concourse import mybir as _mybir
    from concourse.bass_utils import run_bass_kernel_spmd as _run

    nc = _bacc.Bacc("TRN2", target_bir_lowering=False, num_devices=1)
    arrays, args = {}, []
    for name in _INS:
        a = _np.ascontiguousarray(inputs[name])
        arrays[f"in_{name}"] = a
        args.append(nc.dram_tensor(f"in_{name}", a.shape, _mybir.dt.from_np(a.dtype), kind="ExternalInput").ap())
    batch, _, dim = inputs["r_x"].shape
    pairs = inputs["L0_rec_W"].shape[0]
    args.append(nc.dram_tensor("out_dram", (batch, pairs, dim), _mybir.dt.from_np(_np.dtype("float32")),
                               kind="ExternalOutput").ap())
    field_interaction_kernel(nc, *args)
    r = _run(nc, [arrays], core_ids=[0])
    return r.results[0]["out_dram"]
```
